# Optimizing a Trainium2 kernel written in Bass

```python
import numpy as np
import jax
import jax.numpy as jnp

def _softmax(x, axis=-1):
    return jax.nn.softmax(x, axis=axis)

def _gelu(x):
    return jax.nn.gelu(x, approximate=True)

def _silu(x):
    return jax.nn.silu(x)

def _sigmoid(x):
    return jax.nn.sigmoid(x)

def _layernorm(x, axis=-1, eps=1e-05):
    m = jnp.mean(x, axis=axis, keepdims=True)
    v = jnp.var(x, axis=axis, keepdims=True)
    return (x - m) / jnp.sqrt(v + eps)

def _scatter_add(tgt, idx, src, axis=0):
    return tgt.at[idx].add(src)

def _segment_sum(src, seg, n):
    return jax.ops.segment_sum(src, seg, n)
kernel_name = 'mk_adj_ffn_d1_adj_r2_cd109f'

def setup_inputs(seed: int=0):
    np.random.seed(seed)
    _w = jnp.asarray

    def _rec_inputs():
        import jax
        import jax.numpy as jnp
        _gk = jax.random.key(seed)
        x = 7.22e-05 + 1 * jax.random.normal(jax.random.fold_in(_gk, 1), (8, 1024, 128), jnp.float32)
        _a = jax.random.bernoulli(jax.random.fold_in(_gk, 2), 0.00195312, (8, 1024, 1024))
        _a = jnp.logical_or(_a, jnp.eye(1024, dtype=bool))
        _af = _a.astype(jnp.float32)
        _af = _af * jax.random.uniform(jax.random.fold_in(_gk, 3), (8, 1024, 1024), jnp.float32, 0.05, 1)
        adj = _af
        return (x, adj)
    x, adj = _rec_inputs()

    def _L0_gnn_setup():
        import jax, jax.numpy as jnp
        import numpy as np
        D_IN = 128
        D_HID = 256
        key = jax.random.key(seed)
        k1, k2, k3, k4, k5, k6 = jax.random.split(key, 6)
        x = jax.random.normal(k1, (8, 2048, D_IN), dtype=jnp.float32)
        adj = jax.random.uniform(k2, (8, 2048, 2048), dtype=jnp.float32)
        s1 = 1.0 / np.sqrt(D_IN)
        s2 = 1.0 / np.sqrt(D_HID)
        W1 = jax.random.uniform(k3, (D_IN, D_HID), dtype=jnp.float32, minval=-s1, maxval=s1)
        b1 = jax.random.uniform(k4, (D_HID,), dtype=jnp.float32, minval=-s1, maxval=s1)
        W2 = jax.random.uniform(k5, (D_HID, D_IN), dtype=jnp.float32, minval=-s2, maxval=s2)
        b2 = jax.random.uniform(k6, (D_IN,), dtype=jnp.float32, minval=-s2, maxval=s2)
        eps = jnp.zeros((1,), dtype=jnp.float32)
        return {'x': x, 'adj': adj, 'eps': eps, 'W1': W1, 'b1': b1, 'W2': W2, 'b2': b2}
    _L0_gnn_all = _L0_gnn_setup()
    _L0_gnn_in = {k: v for k, v in _L0_gnn_all.items() if k in ('eps', 'W1', 'b1', 'W2', 'b2')}
    del _L0_gnn_all

    def _L0_ffn_setup():
        import jax, jax.numpy as jnp
        import numpy as np
        E, D, H, TOP_K = (6, 128, 128, 2)
        ROUTER_H = D // 2
        key = jax.random.key(seed)
        ks = jax.random.split(key, 12)
        s = 1.0 / np.sqrt(D)
        sh = 1.0 / np.sqrt(H)
        sr = 1.0 / np.sqrt(ROUTER_H)
        return {'features': jax.random.normal(ks[0], (8, 2048, D), dtype=jnp.float32), 'router_w1': jax.random.uniform(ks[1], (D, ROUTER_H), jnp.float32, -s, s), 'router_b1': jnp.zeros((ROUTER_H,), jnp.float32), 'router_w2': jax.random.uniform(ks[2], (ROUTER_H, E), jnp.float32, -sr, sr), 'router_b2': jnp.zeros((E,), jnp.float32), 'expert_w1': jax.random.uniform(ks[3], (E, D, H), jnp.float32, -s, s), 'expert_b1': jnp.zeros((E, H), jnp.float32), 'expert_w2': jax.random.uniform(ks[4], (E, H, H), jnp.float32, -sh, sh), 'expert_b2': jnp.zeros((E, H), jnp.float32), 'expert_w3': jax.random.uniform(ks[5], (E, H, D), jnp.float32, -sh, sh), 'expert_b3': jnp.zeros((E, D), jnp.float32)}
    _L0_ffn_all = _L0_ffn_setup()
    _L0_ffn_in = {k: v for k, v in _L0_ffn_all.items() if k in ('router_w1', 'router_b1', 'router_w2', 'router_b2', 'expert_w1', 'expert_b1', 'expert_w2', 'expert_b2', 'expert_w3', 'expert_b3')}
    del _L0_ffn_all
    return {'x': x, 'adj': adj, 'L0_gnn_eps': _L0_gnn_in['eps'], 'L0_gnn_W1': _L0_gnn_in['W1'], 'L0_gnn_b1': _L0_gnn_in['b1'], 'L0_gnn_W2': _L0_gnn_in['W2'], 'L0_gnn_b2': _L0_gnn_in['b2'], 'L0_ffn_router_w1': _L0_ffn_in['router_w1'], 'L0_ffn_router_b1': _L0_ffn_in['router_b1'], 'L0_ffn_router_w2': _L0_ffn_in['router_w2'], 'L0_ffn_router_b2': _L0_ffn_in['router_b2'], 'L0_ffn_expert_w1': _L0_ffn_in['expert_w1'], 'L0_ffn_expert_b1': _L0_ffn_in['expert_b1'], 'L0_ffn_expert_w2': _L0_ffn_in['expert_w2'], 'L0_ffn_expert_b2': _L0_ffn_in['expert_b2'], 'L0_ffn_expert_w3': _L0_ffn_in['expert_w3'], 'L0_ffn_expert_b3': _L0_ffn_in['expert_b3']}

def reference(x, adj, L0_gnn_eps, L0_gnn_W1, L0_gnn_b1, L0_gnn_W2, L0_gnn_b2, L0_ffn_router_w1, L0_ffn_router_b1, L0_ffn_router_w2, L0_ffn_router_b2, L0_ffn_expert_w1, L0_ffn_expert_b1, L0_ffn_expert_w2, L0_ffn_expert_b2, L0_ffn_expert_w3, L0_ffn_expert_b3):
    import jax
    import jax.numpy as jnp

    def _L0_gnn_ref(x, adj, eps, W1, b1, W2, b2):
        import jax, jax.numpy as jnp
        import numpy as np
        D_IN = 128
        D_HID = 256
        aggregated = jnp.einsum('bnm,bmd->bnd', adj, x)
        h = (1.0 + eps) * x + aggregated
        h = jax.nn.relu(h @ W1 + b1)
        return h @ W2 + b2

    def _L0_ffn_ref(features, router_w1, router_b1, router_w2, router_b2, expert_w1, expert_b1, expert_w2, expert_b2, expert_w3, expert_b3):
        import jax, jax.numpy as jnp
        import numpy as np
        E, D, H, TOP_K = (6, 128, 128, 2)
        ROUTER_H = D // 2
        rh = jax.nn.relu(features @ router_w1 + router_b1)
        expert_logits = jax.nn.softmax(rh @ router_w2 + router_b2, axis=-1)
        top_w, top_i = jax.lax.top_k(expert_logits, TOP_K)
        routing_weights = jax.nn.softmax(top_w, axis=-1)
        h1 = jax.nn.relu(jnp.einsum('bsd,edh->bseh', features, expert_w1) + expert_b1)
        h2 = jax.nn.relu(jnp.einsum('bseh,ehf->bsef', h1, expert_w2) + expert_b2)
        expert_out = jnp.einsum('bsef,efo->bseo', h2, expert_w3) + expert_b3
        sel = jnp.take_along_axis(expert_out, top_i[:, :, :, None], axis=2)
        combined = jnp.sum(sel * routing_weights[..., None], axis=2)
        return combined
    x = x + _L0_gnn_ref(_layernorm(x, axis=-1), adj, L0_gnn_eps, L0_gnn_W1, L0_gnn_b1, L0_gnn_W2, L0_gnn_b2)
    x = x + _L0_ffn_ref(_layernorm(x, axis=-1), L0_ffn_router_w1, L0_ffn_router_b1, L0_ffn_router_w2, L0_ffn_router_b2, L0_ffn_expert_w1, L0_ffn_expert_b1, L0_ffn_expert_w2, L0_ffn_expert_b2, L0_ffn_expert_w3, L0_ffn_expert_b3)
    return x

_drawn_inputs = setup_inputs


def setup_inputs(seed=0):
    import zlib

    import numpy as np

    out = dict(_drawn_inputs(seed))
    spreads = {'L0_ffn_router_b1': (0.0, 0.1),
     'L0_ffn_router_b2': (0.0, 0.1),
     'L0_ffn_expert_b1': (0.0, 0.768),
     'L0_ffn_expert_b2': (0.0, 0.291),
     'L0_ffn_expert_b3': (0.0, 0.1)}
    factors = {}
    for name, (base, spread) in spreads.items():
        noise = np.random.default_rng([zlib.crc32(name.encode()), seed]).standard_normal(out[name].shape)
        drawn = base * np.exp(spread * noise) if base else spread * noise
        out[name] = jnp.asarray(drawn.astype(out[name].dtype))
    for name, factor in factors.items():
        out[name] = (out[name] * factor).astype(out[name].dtype)
    return out
```

```python
from contextlib import ExitStack

import concourse.bass as bass
from concourse import mybir

F32 = mybir.dt.float32
F32R = mybir.dt.float32r
ALU = mybir.AluOpType
ACT = mybir.ActivationFunctionType
AX = mybir.AxisListType.X

P = 128
TN = 512
KT = TN // P
LN_EPS = 1e-5
SEL = 32


def build(nc, x, adj, eps, W1, b1, W2, b2, rw1, rb1, rw2, rb2, ew1, eb1, ew2, eb2, ew3, eb3, out):
    B, N, D = x.shape
    HID = W1.shape[1]
    NH = HID // P
    RH = rw1.shape[1]
    E = ew1.shape[0]
    HALVES = N // TN
    TILES = B * HALVES
    Q = 4
    MB = N // (Q * 32)
    RB = TN // 32
    QC = N // Q
    assert D == P and HALVES == 2 and RH <= P and E * 4 <= SEL

    ctx = ExitStack()
    with ctx:
        def sb(name, shape, dt=F32):
            return ctx.enter_context(nc.sbuf_tensor(name, shape, dt))

        def sem(name):
            return ctx.enter_context(nc.semaphore(name))

        ident = sb("ident", [P, P])
        eps_eye = sb("eps_eye", [P, Q, 32])
        eps_col = sb("eps_col", [P, 1])
        half_neg = sb("half_neg", [P, MB])
        first = sb("first", [P, E])
        zero_col = sb("zero_col", [P, 1])
        W1_raw = sb("W1_raw", [P, HID])
        W1_hi, W1_lo = sb("W1_hi", [P, HID], F32R), sb("W1_lo", [P, HID], F32R)
        W2_sb = sb("W2_sb", [P, NH, P])
        bias_rows = sb("bias_rows", [32, P])
        bias_cols = sb("bias_cols", [P, 32])
        cols, i = {}, 0
        for name, n in (("b1", NH), ("b2", 1), ("rb1", 1), ("eb1", E), ("eb2", E), ("eb3", E)):
            cols[name] = bias_cols[:, i:i + n], slice(i, i + n)
            i += n
        assert i <= 32
        b1_col, b2_col, rb1_col, eb1_col, eb2_col, eb3_col = (c for c, _ in cols.values())
        rw1_raw = sb("rw1_raw", [P, P])
        rw1_hi, rw1_lo = sb("rw1_hi", [P, P], F32R), sb("rw1_lo", [P, P], F32R)
        rw2_sb = sb("rw2_sb", [P, E])
        rb2_row = sb("rb2_row", [P, E])
        e1_raw = sb("e1_raw", [P, E, P])
        e1_hi, e1_lo = sb("e1_hi", [P, E, P], F32R), sb("e1_lo", [P, E, P], F32R)
        e2_sb = sb("e2_sb", [P, E, P])
        e3_sb = sb("e3_sb", [P, E, P])
        neg_eb2 = sb("neg_eb2", [P, E])
        cT = sb("cT", [P, E])
        cT_hi = sb("cT_hi", [P, E], F32R)
        cT_stack = sb("cT_stack", [P, P])
        c_stack = sb("c_stack", [P, P], F32R)

        diag_step = QC + 32
        raw = sb("raw", [P, 2, RB * QC + MB * 32])
        adjT = sb("adjT", [P, 2, MB, TN])
        x_perm = sb("x_perm", [P, MB, P])
        xn = sb("xn", [P, MB, P])
        x_nat = sb("x_nat", [P, 2, KT, P])
        bn1 = sb("bn1", [P, MB, 6])
        mv1 = sb("mv1", [P, MB, 2])
        ve1 = sb("ve1", [P, MB])
        rstd1 = sb("rstd1", [P, MB])
        hT_hi, hT_lo = sb("hT_hi", [P, TN], F32R), sb("hT_lo", [P, TN], F32R)
        h1T = sb("h1T", [P, NH, TN])
        goT = sb("goT", [P, TN])
        x2 = sb("x2", [P, 2, KT, P])
        bn2 = sb("bn2", [P, KT, 6])
        mv2 = sb("mv2", [P, KT, 2])
        ve2 = sb("ve2", [P, KT])
        rstd2 = sb("rstd2", [P, KT])
        xn2 = sb("xn2", [P, KT, P])
        xT_hi, xT_lo = sb("xT_hi", [P, 2, TN], F32R), sb("xT_lo", [P, 2, TN], F32R)
        rhT = sb("rhT", [P, TN])
        lg, lgd, ex, pr, pr2 = (sb(n, [P, KT, E]) for n in ("lg", "lgd", "ex", "pr", "pr2"))
        tie, top1, top2, g1, g2 = (sb(n, [P, KT, E]) for n in ("tie", "top1", "top2", "g1", "g2"))
        mx, sm, m1, m2, kk, dm, ed, den, w1, w2 = (
            sb(n, [P, KT]) for n in ("mx", "sm", "m1", "m2", "kk", "dm", "ed", "den", "w1", "w2"))
        gate_hi = sb("gate_hi", [P, KT, E], F32R)
        gates = sb("gates", [P, KT, P])
        gT_stack = sb("gT_stack", [P, TN], F32R)
        gT = sb("gT", [SEL, TN])
        gate_row = sb("gate_row", [1, E, TN])
        gate_all = sb("gate_all", [P, E, TN])
        h1e = sb("h1e", [P, 2, TN])
        h2e = sb("h2e", [P, 2, TN])
        accT = sb("accT", [P, TN])
        y = sb("y", [P, 2, KT, P])

        bank = [ctx.enter_context(nc.psum_tensor(f"bank{i}", [P, TN], F32)) for i in range(8)]
        z1, z2, acc = bank[0:2], bank[2:4], bank[4]
        FA, FB, FC = bank[5:8]

        s_w = sem("weights_in")
        s_apart = sem("waits_passed")
        s_ident = sem("identity")
        s_setup = sem("setup_dve")
        s_setup_pe = sem("setup_pe")
        s_ready = sem("constants_ready")
        s_raw = [sem("adj_in_even"), sem("adj_in_odd")]
        s_xp = sem("x_perm_in")
        s_xnat = [sem("x_nat_in_even"), sem("x_nat_in_odd")]
        s_out = [sem("y_out_even"), sem("y_out_odd")]
        s_diag = sem("diagonal_added")
        s_tp = sem("adj_transposed")
        s_ln1 = sem("ln1_steps")
        s_ve1 = sem("var1_ready")
        s_rstd1 = sem("rstd1_ready")
        s_xn = sem("xn_ready")
        s_agg = sem("agg_done")
        s_hhi = sem("h_hi_ready")
        s_hlo = sem("h_lo_ready")
        s_g1 = sem("gin1_done")
        s_h1 = sem("h1_ready")
        s_g2 = sem("gin2_done")
        s_go = sem("gin_out_ready")
        s_tr = sem("gin_out_in_rows")
        s_ln2 = sem("ln2_steps")
        s_ve2 = sem("var2_ready")
        s_rstd2 = sem("rstd2_ready")
        s_xn2 = sem("xn2_ready")
        s_tr2 = sem("xn2_transposed")
        s_xhi = sem("xT_hi_ready")
        s_xlo = sem("xT_lo_ready")
        s_rt = sem("router1_done")
        s_rh = sem("router_hidden_ready")
        s_lg = sem("logits_done")
        s_rs = sem("routing_steps")
        s_ex = sem("exp_done")
        s_gates = sem("gates_ready")
        s_gt = sem("gates_transposed")
        s_gte = sem("gates_copied")
        s_grow = sem("gate_row_in")
        s_gb = sem("gates_broadcast")
        s_z1 = sem("expert1_done")
        s_h1e = sem("expert_h1_ready")
        s_z2 = sem("expert2_done")
        s_h2e = sem("expert_h2_ready")
        s_l3 = sem("expert3_done")
        s_acc = sem("experts_summed")
        s_acce = sem("acc_copied")
        s_ft = sem("acc_in_rows")
        s_fin = sem("y_ready")

        def after(t, ahead):
            b, h = t
            return b + (h + ahead) // 2, (h + ahead) % 2

        def at(t, per_tile, more=0):
            b, h = t
            return b * (2 * per_tile) + (per_tile * h + more)

        def over_tiles(engine, body):
            with engine.Fori(0, B - 1) as b:
                body((b, 0), True, True)
                body((b, 1), True, True)
            body((B - 1, 0), True, False)
            body((B - 1, 1), False, False)

        def wait_apart(engine, semaphore, value):
            engine.wait_ge(semaphore, value)
            engine.sem_inc(s_apart)

        class Steps:

            def __init__(self, engine, semaphore, base):
                self.engine, self.semaphore, self.base, self.n = engine, semaphore, base, 0

            def then(self, instruction, apart=False):
                instruction.then_inc(self.semaphore, 1)
                self.n += 1
                if apart:
                    wait_apart(self.engine, self.semaphore, self.base + self.n)
                else:
                    self.engine.wait_ge(self.semaphore, self.base + self.n)

        WEIGHT_LOADS = 7 + 8
        block = ctx.enter_context(nc.Block())

        @block.sync
        def _(sp):
            def load_adj(t):
                b, h = t
                src = adj[b, h * TN:(h + 1) * TN, :].rearrange("(k i) (q c) -> q i k c", i=32, q=Q)
                for q in range(Q):
                    dst = raw[32 * q:32 * q + 32, h, 0:RB * QC].rearrange("p (k c) -> p k c", c=QC)
                    sp.dma_start(dst, src[q]).then_inc(s_raw[h], 16)

            def load_x_perm(b):
                src = x[b].rearrange("(q m j) d -> q j m d", q=Q, m=MB)
                for q in range(Q):
                    sp.dma_start(x_perm[32 * q:32 * q + 32, :, :], src[q]).then_inc(s_xp, 16)

            def load_x_nat(t):
                b, h = t
                sp.dma_start(x_nat[:, h], x[b, h * TN:(h + 1) * TN, :].rearrange("(k p) d -> p k d", p=P)) \
                    .then_inc(s_xnat[h], 16)

            for h in range(2):
                sp.sem_inc(s_out[h], 16)
            load_x_perm(0)
            load_adj((0, 0))
            loads = [
                (eps_col[:, :], eps.rearrange("(a n) -> a n", a=1).broadcast_to([P, 1])),
                (W1_raw[:, :], W1),
                (W2_sb[:, :, :], W2.rearrange("(c p) n -> p c n", p=P)),
                (rb2_row[:, :], rb2.rearrange("(a n) -> a n", a=1).broadcast_to([P, E])),
                (e1_raw[:, :, :], ew1.rearrange("e d h -> d e h")),
                (e2_sb[:, :, :], ew2.rearrange("e d h -> d e h")),
                (e3_sb[:, :, :], ew3.rearrange("e d h -> d e h")),
            ]
            for dst, src in loads:
                sp.dma_start(dst, src).then_inc(s_w, 16)
            sp.wait_ge(s_setup, 3)
            sp.dma_start(rw1_raw[:, 0:RH], rw1).then_inc(s_w, 16)
            rows = {name: bias_rows[where, :] for name, (_, where) in cols.items()}
            sp.dma_start(rows["b1"], b1.rearrange("(c p) -> c p", p=P)).then_inc(s_w, 16)
            sp.dma_start(rows["b2"], b2.rearrange("(a p) -> a p", a=1)).then_inc(s_w, 16)
            sp.dma_start(rows["rb1"][:, 0:RH], rb1.rearrange("(a p) -> a p", a=1)).then_inc(s_w, 16)
            for name, rows_in in (("eb1", eb1), ("eb2", eb2), ("eb3", eb3)):
                sp.dma_start(rows[name], rows_in).then_inc(s_w, 16)
            sp.dma_start(rw2_sb[0:RH, :], rw2).then_inc(s_w, 16)
            load_x_nat((0, 0))
            load_adj((0, 1))
            load_x_nat((0, 1))

            def tile(t, front, prep):
                b, h = t
                if prep:
                    wait_apart(sp, s_tp, at(t, MB, MB))
                    load_adj(after(t, 2))
                    if h == 0:
                        wait_apart(sp, s_xn, b + 1)
                        load_x_perm(b + 1)
                    wait_apart(sp, s_xn2, at(t, 1, 1))
                    load_x_nat(after(t, 2))
                wait_apart(sp, s_gte, at(t, 2, 2))
                wait_apart(sp, s_gb, at(t, E, 1))
                sp.dma_start(gate_row[0:1, :, :], gT[3 * E:4 * E, :]).then_inc(s_grow, 16)
                wait_apart(sp, s_fin, at(t, 1, 2))
                sp.dma_start(out[b, h * TN:(h + 1) * TN, :].rearrange("(k p) d -> p k d", p=P), y[:, h]) \
                    .then_inc(s_out[h], 16)

            over_tiles(sp, tile)
            for h in range(2):
                sp.wait_ge(s_out[h], 16 * B + 16)

        @block.gpsimd
        def _(pool):
            nc.gpsimd.memset(ident[:, :], 0.0).then_inc(s_ident, 1)
            nc.gpsimd.memset(half_neg[:, :], -0.5).then_inc(s_ident, 1)
            pool.wait_ge(s_ident, 2)
            nc.gpsimd.affine_select(out=ident[:, :], in_=ident[:, :], compare_op=ALU.not_equal, fill=1.0,
                                    base=0, pattern=[[-1, P]], channel_multiplier=1).then_inc(s_ident, 1)

            def add_diagonal(t):
                b, h = t
                pool.wait_ge(s_raw[h], b * (16 * Q) + 16 * Q)
                for q in range(2 * h, 2 * h + 2):
                    at0 = (q - 2 * h) * MB * QC
                    d = raw[:, h, at0:at0 + MB * diag_step].rearrange("p (m f) -> p m f", f=diag_step)[:, :, 0:32]
                    e = eps_eye[:, q, :].unsqueeze(1).broadcast_to([P, MB, 32])
                    nc.gpsimd.tensor_tensor(d, d, e, ALU.add).then_inc(s_diag, 1)

            def rsqrt1(b):
                pool.wait_ge(s_ve1, b + 1)
                nc.gpsimd.tensor_tensor(rstd1[:, :], ve1[:, :], half_neg[:, :], ALU.pow).then_inc(s_rstd1, 1)

            def rsqrt2(t):
                pool.wait_ge(s_ve2, at(t, 1, 1))
                nc.gpsimd.tensor_tensor(rstd2[:, :], ve2[:, :], half_neg[:, 0:KT], ALU.pow).then_inc(s_rstd2, 1)

            pool.sem_inc(s_gb, 1)
            rsqrt1(0)
            pool.wait_ge(s_ready, 1)
            add_diagonal((0, 0))
            add_diagonal((0, 1))
            rsqrt2((0, 0))

            def tile(t, front, prep):
                b, h = t
                pool.wait_ge(s_grow, at(t, 16, 16))
                wait_apart(pool, s_h2e, at(t, E, 1))
                for e in range(E):
                    nc.gpsimd.partition_broadcast(gate_all[:, e, :], gate_row[0:1, e, :], P).then_inc(s_gb, 1)
                if prep:
                    add_diagonal(after(t, 2))
                if front:
                    rsqrt2(after(t, 1))
                if prep and h == 0:
                    rsqrt1(b + 1)

            over_tiles(pool, tile)

        def ln_stats(dve, steps, bn, mv, ve, src, n):
            for k in range(n):
                last = nc.vector.bn_stats(bn[:, k, :], src[:, k, :])
            steps.then(last, apart=True)
            for k in range(n):
                last = nc.vector.bn_aggr(mv[:, k, :], bn[:, k, :])
            steps.then(last)
            return nc.vector.tensor_scalar(ve[:, :], mv[:, :, 1], LN_EPS, None, ALU.add)

        LN_STEPS = 2
        ROUTE_STEPS, ROUTE_LESS_MAX, ROUTE_LESS_TOP = 25, 3, 14

        @block.vector
        def _(dve):
            def split(dst_hi, dst_lo, src):
                nc.vector.tensor_copy(dst_hi, src).then_inc(s_setup, 1)
                split.n += 1
                dve.wait_ge(s_setup, split.n)
                return nc.vector.tensor_tensor(dst_lo, src, dst_hi.bitcast(F32), ALU.subtract)

            dve.sem_inc(s_h2e, 1)
            dve.sem_inc(s_fin, 1)
            nc.vector.memset(rw1_raw[:, :], 0.0).then_inc(s_setup, 1)
            nc.vector.memset(bias_rows[:, :], 0.0).then_inc(s_setup, 1)
            nc.vector.memset(rw2_sb[:, :], 0.0).then_inc(s_setup, 1)
            nc.vector.memset(gates[:, :, :], 0.0).then_inc(s_setup, 1)
            nc.vector.memset(cT_stack[:, :], 0.0).then_inc(s_setup, 1)
            for e in range(E):
                nc.vector.memset(first[:, e:e + 1], float(E - e)).then_inc(s_setup, 1)
            split.n = 5 + E

            def transpose_adj(t, m0, m1):
                b, h = t
                for m in range(m0, m1):
                    if m == 0:
                        dve.wait_ge(s_diag, at(t, 2, 2))
                        if not (isinstance(b, int) and b == 0):
                            dve.wait_ge(s_agg, at(t, 1, -1))
                    src = raw[:, h, 0:RB * QC].rearrange("p (k m j) -> p m k j", m=MB, j=32)[:, m]
                    nc.vector.transpose(adjT[:, h, m, :].rearrange("p (k i) -> p k i", i=32), src) \
                        .then_inc(s_tp, 1)

            def ln1_stats(b):
                dve.wait_ge(s_xp, b * (16 * Q) + 16 * Q)
                steps = Steps(dve, s_ln1, b * LN_STEPS)
                ln_stats(dve, steps, bn1, mv1, ve1, x_perm, MB).then_inc(s_ve1, 1)

            def ln1_norm(b):
                dve.wait_ge(s_rstd1, b + 1)
                if not (isinstance(b, int) and b == 0):
                    dve.wait_ge(s_agg, b * 2)
                for m in range(MB):
                    last = nc.vector.tensor_scalar(xn[:, m, :], x_perm[:, m, :], mv1[:, m, 0:1],
                                                   rstd1[:, m:m + 1], ALU.subtract, ALU.mult)
                last.then_inc(s_xn, 1)

            def h_lo(t):
                dve.wait_ge(s_hhi, at(t, 1, 1))
                nc.vector.tensor_tensor(hT_lo[:, :], FA[:, :], hT_hi[:, :].bitcast(F32), ALU.subtract) \
                    .then_inc(s_hlo, 1)

            def x_lo(t):
                dve.wait_ge(s_xhi, at(t, 1, 1))
                nc.vector.tensor_tensor(xT_lo[:, t[1], :], FC[:, :], xT_hi[:, t[1], :].bitcast(F32),
                                        ALU.subtract).then_inc(s_xlo, 1)

            def residual_and_stats(t):
                b, h = t
                dve.wait_ge(s_tr, at(t, 1, 1))
                dve.wait_ge(s_xnat[h], b * 16 + 16)
                steps = Steps(dve, s_ln2, at(t, LN_STEPS + 1))
                steps.then(nc.vector.tensor_tensor(x2[:, h].rearrange("p k d -> p (k d)"), FB[:, :],
                                                   x_nat[:, h].rearrange("p k d -> p (k d)"), ALU.add))
                ln_stats(dve, steps, bn2, mv2, ve2, x2[:, h], KT).then_inc(s_ve2, 1)
                assert steps.n == LN_STEPS + 1

            def norm2(t):
                h = t[1]
                dve.wait_ge(s_rstd2, at(t, 1, 1))
                for k in range(KT):
                    last = nc.vector.tensor_scalar(xn2[:, k, :], x2[:, h, k, :], mv2[:, k, 0:1],
                                                   rstd2[:, k:k + 1], ALU.subtract, ALU.mult)
                last.then_inc(s_xn2, 1)

            def expert_gate(t, e):
                dve.wait_ge(s_z2, at(t, E, e + 1))
                dve.wait_ge(s_gb, at(t, E, e + 2))
                if e >= 2:
                    dve.wait_ge(s_l3, at(t, E, e - 1))
                nc.vector.scalar_tensor_tensor(out=h2e[:, e % 2, :], in0=z2[e % 2][:, :],
                                               scalar=neg_eb2[:, e:e + 1], in1=gate_all[:, e, :],
                                               op0=ALU.max, op1=ALU.mult).then_inc(s_h2e, 1)

            def finish(t):
                b, h = t
                dve.wait_ge(s_ft, at(t, 1, 1))
                dve.wait_ge(s_out[h], b * 16 + 16)
                nc.vector.tensor_tensor(y[:, h].rearrange("p k d -> p (k d)"), FB[:, :],
                                        x2[:, h].rearrange("p k d -> p (k d)"), ALU.add).then_inc(s_fin, 1)

            def wide(v):
                return v.unsqueeze(2).broadcast_to([P, KT, E])

            def route(t, between=None):
                TT, v = nc.vector.tensor_tensor, nc.vector
                steps = Steps(dve, s_rs, at(t, ROUTE_STEPS))
                dve.wait_ge(s_lg, at(t, 1, 1))
                firsts = first[:, :].unsqueeze(1).broadcast_to([P, KT, E])
                bias = rb2_row[:, :].unsqueeze(1).broadcast_to([P, KT, E])
                steps.then(TT(lg[:, :, :], FB[:, 0:KT * E].rearrange("p (k e) -> p k e", e=E), bias, ALU.add))
                steps.then(v.reduce_max(mx[:, :], lg[:, :, :], AX))
                steps.then(TT(lgd[:, :, :], lg[:, :, :], wide(mx[:, :]), ALU.subtract))
                if between is not None:
                    between()
                dve.wait_ge(s_ex, at(t, 2, 1))
                steps.then(v.reduce_sum(sm[:, :], ex[:, :, :], AX))
                steps.then(v.reciprocal(den[:, :], sm[:, :]))
                steps.then(TT(pr[:, :, :], ex[:, :, :], wide(den[:, :]), ALU.mult))
                steps.then(v.reduce_max(m1[:, :], pr[:, :, :], AX))

                def pick(dst, probs, top):
                    steps.then(TT(tie[:, :, :], probs, wide(top), ALU.is_equal))
                    steps.then(TT(tie[:, :, :], tie[:, :, :], firsts, ALU.mult))
                    steps.then(v.reduce_max(kk[:, :], tie[:, :, :], AX))
                    return TT(dst, tie[:, :, :], wide(kk[:, :]), ALU.is_equal)

                steps.then(pick(top1[:, :, :], pr[:, :, :], m1[:, :]))
                steps.then(v.scalar_tensor_tensor(out=pr2[:, :, :], in0=top1[:, :, :], scalar=-4.0,
                                                  in1=pr[:, :, :], op0=ALU.mult, op1=ALU.add))
                steps.then(v.reduce_max(m2[:, :], pr2[:, :, :], AX))
                steps.then(TT(dm[:, :], m2[:, :], m1[:, :], ALU.subtract))
                steps.then(pick(top2[:, :, :], pr2[:, :, :], m2[:, :]))
                return steps

            def route_end(t, steps):
                TT, v = nc.vector.tensor_tensor, nc.vector
                dve.wait_ge(s_ex, at(t, 2, 2))
                steps.then(v.tensor_scalar(den[:, :], ed[:, :], 1.0, None, ALU.add))
                steps.then(v.reciprocal(w1[:, :], den[:, :]))
                steps.then(TT(w2[:, :], ed[:, :], w1[:, :], ALU.mult))
                steps.then(TT(g1[:, :, :], top1[:, :, :], wide(w1[:, :]), ALU.mult))
                steps.then(TT(g2[:, :, :], top2[:, :, :], wide(w2[:, :]), ALU.mult))
                steps.then(TT(gates[:, :, 3 * E:4 * E], g1[:, :, :], g2[:, :, :], ALU.add))
                steps.then(v.tensor_copy(gate_hi[:, :, :], gates[:, :, 3 * E:4 * E]))
                v.tensor_copy(gates[:, :, 0:E], gate_hi[:, :, :].bitcast(F32))
                v.tensor_copy(gates[:, :, 2 * E:3 * E], gate_hi[:, :, :].bitcast(F32))
                TT(gates[:, :, E:2 * E], gates[:, :, 3 * E:4 * E], gate_hi[:, :, :].bitcast(F32),
                   ALU.subtract).then_inc(s_gates, 1)
                assert steps.n == ROUTE_STEPS, steps.n

            ln1_stats(0)
            dve.wait_ge(s_w, 16 * WEIGHT_LOADS)
            dve.wait_ge(s_setup, split.n)
            dve.wait_ge(s_ident, 3)
            nc.vector.tensor_scalar(eps_col[:, :], eps_col[:, :], 1.0, None, ALU.add).then_inc(s_setup, 1)
            split.n += 1
            dve.wait_ge(s_setup, split.n)
            nc.vector.tensor_scalar(eps_eye[:, :, :].rearrange("p q j -> p (q j)"), ident[:, :], eps_col[:, 0:1], None, ALU.mult) \
                .then_inc(s_ready, 1)
            ln1_norm(0)
            dve.wait_ge(s_setup_pe, 1)
            nc.vector.tensor_copy(bias_cols[:, :], FC[:, 0:32]).then_inc(s_setup, 1)
            split.n += 1
            dve.wait_ge(s_setup, split.n)
            nc.vector.tensor_scalar(neg_eb2[:, :], eb2_col, -1.0, None, ALU.mult).then_inc(s_ready, 1)
            split(W1_hi[:, :], W1_lo[:, :], W1_raw[:, :])
            split(rw1_hi[:, :], rw1_lo[:, :], rw1_raw[:, :])
            split(e1_hi[:, :, :], e1_lo[:, :, :], e1_raw[:, :, :])
            dve.wait_ge(s_setup_pe, 2)
            nc.vector.tensor_tensor(cT[:, :], FC[:, 0:E], eb3_col, ALU.add).then_inc(s_setup, 1)
            split.n += 1
            dve.wait_ge(s_setup, split.n)
            split(cT_hi[:, :], cT_stack[:, 2 * E:3 * E], cT[:, :])
            nc.vector.tensor_copy(cT_stack[:, 0:E], cT_hi[:, :].bitcast(F32))
            nc.vector.tensor_copy(cT_stack[:, E:2 * E], cT_hi[:, :].bitcast(F32)).then_inc(s_ready, 1)
            dve.wait_ge(s_setup_pe, 3)
            nc.vector.tensor_copy(c_stack[:, :], FC[:, 0:P]).then_inc(s_ready, 1)

            transpose_adj((0, 0), 0, MB)
            h_lo((0, 0))
            transpose_adj((0, 1), 0, MB)
            residual_and_stats((0, 0))
            norm2((0, 0))
            x_lo((0, 0))
            route_end((0, 0), route((0, 0)))

            def tile(t, front, prep):
                b, h = t
                f, p2 = after(t, 1), after(t, 2)
                if front:
                    h_lo(f)
                expert_gate(t, 0)
                if prep:
                    transpose_adj(p2, 0, 2)
                expert_gate(t, 1)
                if prep:
                    transpose_adj(p2, 2, 3)
                expert_gate(t, 2)
                if prep:
                    transpose_adj(p2, 3, 4)
                if front:
                    residual_and_stats(f)
                expert_gate(t, 3)
                if front:
                    norm2(f)
                if prep:
                    transpose_adj(p2, 4, 5)
                expert_gate(t, 4)
                if prep:
                    if h == 0:
                        ln1_stats(b + 1)
                    transpose_adj(p2, 5, 6)
                if front:
                    x_lo(f)
                expert_gate(t, 5)
                if prep:
                    if h == 0:
                        ln1_norm(b + 1)
                    transpose_adj(p2, 6, MB)
                if front:
                    steps = route(f, lambda: finish(t))
                    route_end(f, steps)
                else:
                    finish(t)

            over_tiles(dve, tile)

        @block.scalar
        def _(act):
            def h_hi(t):
                act.wait_ge(s_agg, at(t, 1, 1))
                nc.scalar.activation(hT_hi[:, :], FA[:, :], ACT.Copy).then_inc(s_hhi, 1)

            def h1(t):
                for c in range(NH):
                    act.wait_ge(s_g1, at(t, NH, c + 1))
                    nc.scalar.activation(h1T[:, c, :], (FB, FC)[c][:, :], ACT.Relu, bias=b1_col[:, c:c + 1]) \
                        .then_inc(s_h1, 1)

            def gin_out(t):
                act.wait_ge(s_g2, at(t, 1, 1))
                nc.scalar.activation(goT[:, :], FA[:, :], ACT.Identity, bias=b2_col[:, 0:1]).then_inc(s_go, 1)

            def x_hi(t):
                act.wait_ge(s_tr2, at(t, 1, 1))
                nc.scalar.activation(xT_hi[:, t[1], :], FC[:, :], ACT.Copy).then_inc(s_xhi, 1)

            def router_hidden(t):
                act.wait_ge(s_rt, at(t, 1, 1))
                nc.scalar.activation(rhT[:, :], FA[:, :], ACT.Relu, bias=rb1_col[:, 0:1]).then_inc(s_rh, 1)

            def exps(t):
                act.wait_ge(s_rs, at(t, ROUTE_STEPS, ROUTE_LESS_MAX))
                nc.scalar.activation(ex[:, :, :], lgd[:, :, :], ACT.Exp).then_inc(s_ex, 1)
                act.wait_ge(s_rs, at(t, ROUTE_STEPS, ROUTE_LESS_TOP))
                nc.scalar.activation(ed[:, :], dm[:, :], ACT.Exp).then_inc(s_ex, 1)

            def copy_gates(t):
                act.wait_ge(s_gt, at(t, 1, 1))
                nc.scalar.activation(gT_stack[:, :], FC[:, :], ACT.Copy).then_inc(s_gte, 1)
                act.wait_ge(s_gb, at(t, E, 1))
                nc.scalar.activation(gT[:, :], FC[0:SEL, :], ACT.Copy).then_inc(s_gte, 1)

            def expert_h1(t, e):
                act.wait_ge(s_z1, at(t, E, e + 1))
                if e >= 2:
                    act.wait_ge(s_z2, at(t, E, e - 1))
                nc.scalar.activation(h1e[:, e % 2, :], z1[e % 2][:, :], ACT.Relu, bias=eb1_col[:, e:e + 1]) \
                    .then_inc(s_h1e, 1)

            def copy_acc(t):
                act.wait_ge(s_acc, at(t, 1, 1))
                nc.scalar.activation(accT[:, :], acc[:, :], ACT.Copy).then_inc(s_acce, 1)

            act.wait_ge(s_ready, 2)
            h_hi((0, 0))
            h1((0, 0))
            gin_out((0, 0))
            x_hi((0, 0))
            router_hidden((0, 0))
            exps((0, 0))
            expert_h1((0, 0), 0)

            def tile(t, front, prep):
                f = after(t, 1)
                copy_gates(t)
                if front:
                    h_hi(f)
                expert_h1(t, 1)
                if front:
                    h1(f)
                expert_h1(t, 2)
                if front:
                    gin_out(f)
                expert_h1(t, 3)
                expert_h1(t, 4)
                expert_h1(t, 5)
                if front:
                    x_hi(f)
                    router_hidden(f)
                copy_acc(t)
                if front:
                    exps(f)
                    expert_h1(f, 0)

            over_tiles(act, tile)

        @block.tensor
        def _(pe):
            mm = nc.tensor.matmul

            def three_pass(dst, w_hi, w_lo, m_hi, m_lo):
                mm(dst, w_lo, m_hi, start=True, stop=False)
                mm(dst, w_hi, m_lo, start=False, stop=False)
                return mm(dst, w_hi, m_hi, start=False, stop=True)

            def aggregate(t, m0, m1):
                b, h = t
                if m0 == 0 and h == 0:
                    pe.wait_ge(s_xn, b + 1)
                for m in range(m0, m1):
                    pe.wait_ge(s_tp, at(t, MB, m + 1))
                    last = mm(FA[:, :], xn[:, m, :], adjT[:, h, m, :], start=(m == 0), stop=(m == MB - 1))
                if m1 == MB:
                    last.then_inc(s_agg, 1)

            def gin1(t):
                pe.wait_ge(s_hlo, at(t, 1, 1))
                for c in range(NH):
                    w = slice(c * P, (c + 1) * P)
                    three_pass((FB, FC)[c][:, :], W1_hi[:, w], W1_lo[:, w], hT_hi[:, :], hT_lo[:, :]) \
                        .then_inc(s_g1, 1)

            def gin2(t):
                for c in range(NH):
                    pe.wait_ge(s_h1, at(t, NH, c + 1))
                    last = mm(FA[:, :], W2_sb[:, c, :], h1T[:, c, :], start=(c == 0), stop=(c == NH - 1))
                last.then_inc(s_g2, 1)

            def transposes(dst, src):
                for k in range(KT):
                    last = nc.tensor.transpose(dst[:, k * P:(k + 1) * P], src(k), ident[:, :])
                return last

            def gin_out_rows(t):
                pe.wait_ge(s_go, at(t, 1, 1))
                transposes(FB, lambda k: goT[:, k * P:(k + 1) * P]).then_inc(s_tr, 1)

            def xn2_transposed(t):
                pe.wait_ge(s_xn2, at(t, 1, 1))
                transposes(FC, lambda k: xn2[:, k, :]).then_inc(s_tr2, 1)

            def router1(t):
                h = t[1]
                pe.wait_ge(s_xlo, at(t, 1, 1))
                three_pass(FA[:, :], rw1_hi[:, :], rw1_lo[:, :], xT_hi[:, h, :], xT_lo[:, h, :]).then_inc(s_rt, 1)

            def logits(t):
                pe.wait_ge(s_rh, at(t, 1, 1))
                for k in range(KT):
                    last = mm(FB[:, k * E:(k + 1) * E], rhT[:, k * P:(k + 1) * P], rw2_sb[:, :],
                              start=True, stop=True)
                last.then_inc(s_lg, 1)

            def gates_transposed(t):
                pe.wait_ge(s_gates, at(t, 1, 1))
                transposes(FC, lambda k: gates[:, k, :]).then_inc(s_gt, 1)

            def expert1(t, e):
                h = t[1]
                if e >= 2:
                    pe.wait_ge(s_h1e, at(t, E, e - 1))
                three_pass(z1[e % 2][:, :], e1_hi[:, e, :], e1_lo[:, e, :], xT_hi[:, h, :], xT_lo[:, h, :]) \
                    .then_inc(s_z1, 1)

            def expert2(t, e):
                pe.wait_ge(s_h1e, at(t, E, e + 1))
                if e >= 2:
                    pe.wait_ge(s_h2e, at(t, E, e))
                mm(z2[e % 2][:, :], e2_sb[:, e, :], h1e[:, e % 2, :], start=True, stop=True).then_inc(s_z2, 1)

            def expert3(t, e):
                pe.wait_ge(s_h2e, at(t, E, e + 2))
                mm(acc[:, :], e3_sb[:, e, :], h2e[:, e % 2, :], start=(e == 0), stop=False).then_inc(s_l3, 1)

            def expert_biases(t):
                pe.wait_ge(s_gte, at(t, 2, 1))
                mm(acc[:, :], c_stack[:, :], gT_stack[:, :], start=False, stop=True).then_inc(s_acc, 1)

            def acc_rows(t):
                pe.wait_ge(s_acce, at(t, 1, 1))
                transposes(FB, lambda k: accT[:, k * P:(k + 1) * P]).then_inc(s_ft, 1)

            pe.wait_ge(s_ident, 3)
            pe.wait_ge(s_w, 16 * WEIGHT_LOADS)
            nc.tensor.transpose(FC[:, 0:32], bias_rows[:, :], ident[0:32, 0:32]).then_inc(s_setup_pe, 1)
            pe.wait_ge(s_ready, 2)
            for e in range(E):
                last = mm(FC[:, e:e + 1], e3_sb[:, e, :], eb2_col[:, e:e + 1], start=True, stop=True)
            last.then_inc(s_setup_pe, 1)
            pe.wait_ge(s_ready, 3)
            nc.tensor.transpose(FC[:, 0:P], cT_stack[:, :], ident[:, :]).then_inc(s_setup_pe, 1)

            aggregate((0, 0), 0, MB)
            pe.wait_ge(s_ready, 4)
            gin1((0, 0))
            gin2((0, 0))
            gin_out_rows((0, 0))
            xn2_transposed((0, 0))
            router1((0, 0))
            logits((0, 0))
            expert1((0, 0), 0)

            def tile(t, front, prep):
                f = after(t, 1)
                if front:
                    aggregate(f, 0, 6)
                gates_transposed(t)
                if front:
                    aggregate(f, 6, MB)
                expert1(t, 1)
                expert2(t, 0)
                if front:
                    pe.wait_ge(s_fin, at(t, 1, 1))
                    pe.wait_ge(s_gte, at(t, 2, 2))
                    gin1(f)
                expert1(t, 2)
                expert2(t, 1)
                expert3(t, 0)
                if front:
                    gin2(f)
                expert1(t, 3)
                expert2(t, 2)
                expert3(t, 1)
                if front:
                    gin_out_rows(f)
                expert1(t, 4)
                expert2(t, 3)
                expert3(t, 2)
                expert1(t, 5)
                expert2(t, 4)
                expert3(t, 3)
                if front:
                    xn2_transposed(f)
                expert2(t, 5)
                expert3(t, 4)
                if front:
                    router1(f)
                expert3(t, 5)
                expert_biases(t)
                if front:
                    logits(f)
                    expert1(f, 0)
                    pe.wait_ge(s_rs, at(f, ROUTE_STEPS, 1))
                acc_rows(t)

            over_tiles(pe, tile)


_INS = ["x", "adj", "L0_gnn_eps", "L0_gnn_W1", "L0_gnn_b1", "L0_gnn_W2", "L0_gnn_b2",
        "L0_ffn_router_w1", "L0_ffn_router_b1", "L0_ffn_router_w2", "L0_ffn_router_b2",
        "L0_ffn_expert_w1", "L0_ffn_expert_b1", "L0_ffn_expert_w2", "L0_ffn_expert_b2",
        "L0_ffn_expert_w3", "L0_ffn_expert_b3"]


def kernel(**inputs):
    import numpy as np
    import concourse.bacc as bacc
    from concourse.bass_utils import run_bass_kernel_spmd

    nc = bacc.Bacc("TRN2", target_bir_lowering=False, num_devices=1)
    arrays, args = {}, []
    for name in _INS:
        a = np.ascontiguousarray(inputs[name])
        arrays[name] = a
        args.append(nc.dram_tensor(name, a.shape, mybir.dt.from_np(a.dtype), kind="ExternalInput").ap())
    y = nc.dram_tensor("y_out", arrays["x"].shape, F32, kind="ExternalOutput").ap()
    build(nc, *args, y)
    r = run_bass_kernel_spmd(nc, [arrays], core_ids=[0])
    return r.results[0]["y_out"]
```

```python
from contextlib import ExitStack

import concourse.bass as bass
from concourse import mybir

F32 = mybir.dt.float32
F32R = mybir.dt.float32r
ALU = mybir.AluOpType
ACT = mybir.ActivationFunctionType
AX = mybir.AxisListType.X

P = 128
TN = 512
KT = TN // P
LN_EPS = 1e-5
SEL = 32


def build(nc, x, adj, eps, W1, b1, W2, b2, rw1, rb1, rw2, rb2, ew1, eb1, ew2, eb2, ew3, eb3, out):
    B, N, D = x.shape
    HID = W1.shape[1]
    NH = HID // P
    RH = rw1.shape[1]
    E = ew1.shape[0]
    HALVES = N // TN
    Q = 4
    MB = N // (Q * 32)
    RB = TN // 32
    QC = N // Q
    assert D == P and HALVES == 2 and RH <= P and E * 4 <= SEL and E % 2 == 0

    ctx = ExitStack()
    with ctx:
        RING = 4
        EH = E // 2

        def sb(name, shape, dt=F32):
            return ctx.enter_context(nc.sbuf_tensor(name, shape, dt))

        def sem(name):
            return ctx.enter_context(nc.semaphore(name))

        ident = sb("ident", [P, P])
        eps_eye = sb("eps_eye", [P, Q, 32])
        eps_col = sb("eps_col", [P, 1])
        half_neg = sb("half_neg", [P, MB])
        numbers = sb("numbers", [P, E])
        pick_first = sb("pick_first", [P, P], F32R)
        W1_hi, W1_lo = sb("W1_hi", [P, HID], F32R), sb("W1_lo", [P, HID], F32R)
        W2_sb = sb("W2_sb", [P, NH, P])
        bias_rows = sb("bias_rows", [32, P])
        bias_cols = sb("bias_cols", [P, 32])
        cols, i = {}, 0
        for name, n in (("b1", NH), ("rb1", 1), ("eb1", E), ("eb2", E), ("eb3", E)):
            cols[name] = bias_cols[:, i:i + n], slice(i, i + n)
            i += n
        assert i <= 32
        b1_col, rb1_col, eb1_col, eb2_col, eb3_col = (c for c, _ in cols.values())
        rw1_hi, rw1_lo = sb("rw1_hi", [P, P], F32R), sb("rw1_lo", [P, P], F32R)
        rw2_sb = sb("rw2_sb", [P, E])
        b2_row = sb("b2_row", [P, P])
        rb2_row = sb("rb2_row", [P, E])
        e1_hi, e1_lo = sb("e1_hi", [P, E, P], F32R), sb("e1_lo", [P, E, P], F32R)
        e2_hi, e2_lo = sb("e2_hi", [P, E, P], F32R), sb("e2_lo", [P, E, P], F32R)
        e3_sb = sb("e3_sb", [P, E, P])
        neg_eb2 = sb("neg_eb2", [P, E])
        cT = sb("cT", [P, E])
        cT_hi = sb("cT_hi", [P, E], F32R)
        cT_stack = sb("cT_stack", [P, P])
        c_stack = sb("c_stack", [P, P], F32R)

        diag_step = QC + 32
        raw = sb("raw", [P, 2, RB * QC + MB * 32])
        adjT = sb("adjT", [P, RING, TN])
        OWN = MB // 2
        adj_hi, adj_lo = (sb(n, [P, MB + OWN, TN], F32R) for n in ("adj_hi", "adj_lo"))
        x_perm = sb("x_perm", [P, MB, P])
        xn_hi, xn_lo = sb("xn_hi", [P, MB, P], F32R), sb("xn_lo", [P, MB, P], F32R)
        x_nat = sb("x_nat", [P, 2, KT, P])
        bn1 = sb("bn1", [P, MB, 6])
        mv1 = sb("mv1", [P, MB, 2])
        ve1 = sb("ve1", [P, MB])
        rstd1 = sb("rstd1", [P, MB])
        hT_hi, hT_lo = sb("hT_hi", [P, TN], F32R), sb("hT_lo", [P, TN], F32R)
        h1T = sb("h1T", [P, NH, TN])
        x2 = sb("x2", [P, 2, KT, P])
        bn2 = sb("bn2", [P, KT, 6])
        mv2 = sb("mv2", [P, KT, 2])
        ve2 = sb("ve2", [P, KT])
        rstd2 = sb("rstd2", [P, KT])
        xn2 = sb("xn2", [P, KT, P])
        xT_hi, xT_lo = sb("xT_hi", [P, 2, TN], F32R), sb("xT_lo", [P, 2, TN], F32R)
        rhT = sb("rhT", [P, TN])
        lg, lgd, ex, top1, top2, g1, g2 = (
            sb(n, [P, KT, E]) for n in ("lg", "lgd", "ex", "top1", "top2", "g1", "g2"))
        mx, sm, inv, dm, ed, den, w1, w2 = (
            sb(n, [P, KT]) for n in ("mx", "sm", "inv", "dm", "ed", "den", "w1", "w2"))
        pr = sb("pr", [P, KT, 8])
        best = sb("best", [P, KT, 8])
        best_at = sb("best_at", [P, KT, 8], mybir.dt.uint32)
        gate_hi = sb("gate_hi", [P, KT, E], F32R)
        gates = sb("gates", [P, KT, P])
        gT_stack = sb("gT_stack", [P, TN], F32R)
        gT = sb("gT", [SEL, TN])
        gate_row = sb("gate_row", [1, EH, TN])
        gate_all = sb("gate_all", [P, E, TN])
        e1_raw, e2_raw = (gate_all[:, i:i + 2, :].rearrange("p e n -> p (e n)")[:, 0:E * P]
                          .rearrange("p (e h) -> p e h", e=E) for i in (0, 4))
        W1_raw, rw1_raw = gate_all[:, 2, 0:HID], gate_all[:, 3, 0:P]
        h1e = sb("h1e", [P, 2, TN])
        h1e_hi, h1e_lo = sb("h1e_hi", [P, 2, TN], F32R), sb("h1e_lo", [P, 2, TN], F32R)
        h2e = sb("h2e", [P, 2, TN])
        accT = sb("accT", [P, TN])
        y = sb("y", [P, 2, KT, P])

        bank = [ctx.enter_context(nc.psum_tensor(f"bank{i}", [P, TN], F32)) for i in range(8)]
        z1, z2, acc = bank[0:2], bank[2:4], bank[4]
        FA, FB, FC = bank[5:8]

        s_wraw = sem("weights_to_split_in")
        s_w = sem("weights_in")
        s_clear = sem("paddings_cleared")
        s_whi = sem("weight_hi_ready")
        s_wlo = sem("weight_lo_ready")
        s_brow = sem("biases_in")
        s_bias = sem("bias_columns_ready")
        s_c = sem("bias_terms")
        s_apart = sem("waits_passed")
        s_eps = sem("eps_in")
        s_ident = sem("identity")
        s_setup = sem("setup_dve")
        s_setup_pe = sem("setup_pe")
        s_eye = sem("eps_eye_ready")
        s_raw = [sem("adj_in_even"), sem("adj_in_odd")]
        s_xp = sem("x_perm_in")
        s_xnat = [sem("x_nat_in_even"), sem("x_nat_in_odd")]
        s_out = [sem("y_out_even"), sem("y_out_odd")]
        s_diag = sem("diagonal_added")
        s_tp = sem("adj_transposed")
        s_ln1 = sem("ln1_steps")
        s_ve1 = sem("var1_ready")
        s_rstd1 = sem("rstd1_ready")
        s_norm1 = sem("x_normed")
        s_xnhi = sem("xn_hi_ready")
        s_xn = sem("xn_ready")
        s_adjhi = sem("adj_hi_ready")
        s_adjlo = sem("adj_lo_ready")
        s_adjlo0 = sem("adj_lo_of_tile_0")
        s_agg = sem("agg_done")
        s_hhi = sem("h_hi_ready")
        s_hlo = sem("h_lo_ready")
        s_g1 = sem("gin1_done")
        s_h1 = sem("h1_ready")
        s_g2 = sem("gin2_done")
        s_xb = sem("x_plus_b2_ready")
        s_ln2 = sem("ln2_steps")
        s_ve2 = sem("var2_ready")
        s_rstd2 = sem("rstd2_ready")
        s_xn2 = sem("xn2_ready")
        s_tr2 = sem("xn2_transposed")
        s_xhi = sem("xT_hi_ready")
        s_xlo = sem("xT_lo_ready")
        s_rt = sem("router1_done")
        s_rh = sem("router_hidden_ready")
        s_lg = sem("logits_done")
        s_rs = sem("routing_steps")
        s_lgd = sem("less_max_ready")
        s_dm = sem("top_two_subtracted")
        s_ex = sem("exp_done")
        s_gates = sem("gates_ready")
        s_gt = sem("gates_transposed")
        s_gst = sem("gate_halves_copied")
        s_gte = sem("gates_copied")
        s_grow = sem("gate_row_in")
        s_gb = sem("gates_broadcast")
        s_pick = sem("first_gate_spread")
        s_g0 = sem("first_gate_ready")
        s_z1 = sem("expert1_done")
        s_h1e = sem("expert_h1_ready")
        s_h1lo = {"dve": sem("expert_h1_lo_dve"), "pool": sem("expert_h1_lo_pool")}
        s_z2 = sem("expert2_done")
        s_h2e = sem("expert_h2_ready")
        s_l3 = sem("expert3_done")
        s_acc = sem("experts_summed")
        s_acce = sem("acc_copied")
        s_ft = sem("acc_in_rows")
        s_fin = sem("y_ready")

        def after(t, ahead):
            b, h = t
            return b + (h + ahead) // 2, (h + ahead) % 2

        def at(t, per_tile, more=0):
            b, h = t
            return b * (2 * per_tile) + (per_tile * h + more)

        def in_first_graph(t):
            return isinstance(t[0], int) and t[0] == 0

        LOW_BY = ("dve", "pool", "dve", "pool", "dve", "dve")

        def h1_low_done(t, e):
            who = LOW_BY[e]
            return s_h1lo[who], at(t, LOW_BY.count(who), LOW_BY[:e + 1].count(who))

        def slot(t, m):
            return t[1] * OWN + m if m < OWN else OWN + m

        def exists(t):
            return not isinstance(t[0], int) or t[0] < B

        def over_tiles(engine, body):
            with engine.Fori(0, B - 2) as b:
                body((b, 0), True, True)
                body((b, 1), True, True)
            for b in (B - 2, B - 1):
                for h in range(HALVES):
                    body((b, h), exists(after((b, h), 1)), exists(after((b, h), 2)))

        def wait_apart(engine, semaphore, value):
            engine.wait_ge(semaphore, value)
            engine.sem_inc(s_apart)

        class Steps:

            def __init__(self, engine, semaphore, base):
                self.engine, self.semaphore, self.base, self.n = engine, semaphore, base, 0

            def then(self, instruction, apart=False, beside=None):
                instruction.then_inc(self.semaphore, 1)
                self.n += 1
                if beside is not None:
                    beside()
                if apart:
                    wait_apart(self.engine, self.semaphore, self.base + self.n)
                else:
                    self.engine.wait_ge(self.semaphore, self.base + self.n)

        def add_diagonal(engine, t):
            b, h = t
            engine.wait_ge(s_raw[h], b * (16 * Q) + 16 * Q)
            for q in range(2 * h, 2 * h + 2):
                at0 = (q - 2 * h) * MB * QC
                d = raw[:, h, at0:at0 + MB * diag_step].rearrange("p (m f) -> p m f", f=diag_step)[:, :, 0:32]
                e = eps_eye[:, q, :].unsqueeze(1).broadcast_to([P, MB, 32])
                engine.tensor_tensor(d, d, e, ALU.add).then_inc(s_diag, 1)

        BIAS_LOADS, WEIGHT_LOADS = 5, 5
        block = ctx.enter_context(nc.Block())

        @block.sync
        def _(sp):
            def load_adj(t):
                b, h = t
                src = adj[b, h * TN:(h + 1) * TN, :].rearrange("(k i) (q c) -> q i k c", i=32, q=Q)
                for q in range(Q):
                    dst = raw[32 * q:32 * q + 32, h, 0:RB * QC].rearrange("p (k c) -> p k c", c=QC)
                    sp.dma_start(dst, src[q]).then_inc(s_raw[h], 16)

            def load_x_perm(b):
                src = x[b].rearrange("(q m j) d -> q j m d", q=Q, m=MB)
                for q in range(Q):
                    sp.dma_start(x_perm[32 * q:32 * q + 32, :, :], src[q]).then_inc(s_xp, 16)

            def load_x_nat(t):
                b, h = t
                sp.dma_start(x_nat[:, h], x[b, h * TN:(h + 1) * TN, :].rearrange("(k p) d -> p k d", p=P)) \
                    .then_inc(s_xnat[h], 16)

            for h in range(2):
                sp.sem_inc(s_out[h], 16)
            load_x_perm(0)
            sp.dma_start(eps_col[:, :], eps.rearrange("(a n) -> a n", a=1).broadcast_to([P, 1])).then_inc(s_eps, 16)
            load_adj((0, 0))
            sp.dma_start(W1_raw, W1).then_inc(s_wraw, 16)
            sp.wait_ge(s_clear, 3)
            sp.dma_start(rw1_raw[:, 0:RH], rw1).then_inc(s_wraw, 16)
            rows = {name: bias_rows[where, :] for name, (_, where) in cols.items()}
            loads = [
                (rows["b1"], b1.rearrange("(c p) -> c p", p=P)),
                (rows["rb1"][:, 0:RH], rb1.rearrange("(a p) -> a p", a=1)),
                (rows["eb1"], eb1), (rows["eb2"], eb2), (rows["eb3"], eb3),
                (e1_raw, ew1.rearrange("e d h -> d e h")),
                (e2_raw, ew2.rearrange("e d h -> d e h")),
                (W2_sb[:, :, :], W2.rearrange("(c p) n -> p c n", p=P)),
                (rw2_sb[0:RH, :], rw2),
                (rb2_row[:, :], rb2.rearrange("(a n) -> a n", a=1).broadcast_to([P, E])),
                (e3_sb[:, :, :], ew3.rearrange("e d h -> d e h")),
                (b2_row[:, :], b2.rearrange("(a n) -> a n", a=1).broadcast_to([P, P])),
            ]
            for dst, src in loads[:BIAS_LOADS]:
                sp.dma_start(dst, src).then_inc(s_brow, 16)
            for dst, src in loads[BIAS_LOADS:BIAS_LOADS + 2]:
                sp.dma_start(dst, src).then_inc(s_wraw, 16)
            for dst, src in loads[BIAS_LOADS + 2:]:
                sp.dma_start(dst, src).then_inc(s_w, 16)
            load_x_nat((0, 0))
            load_adj((0, 1))
            load_x_nat((0, 1))
            sp.wait_ge(s_tp, MB)
            load_adj((1, 0))
            sp.wait_ge(s_xn, 1)
            load_x_perm(1)

            def tile(t, front, prep):
                b, h = t
                wait_apart(sp, s_gte, at(t, 1, 1))
                wait_apart(sp, s_gb, at(t, E - 1, 1))
                sp.dma_start(gate_row[0:1, :, :], gT[3 * E + 1:3 * E + 1 + EH, :]).then_inc(s_grow, 16)
                wait_apart(sp, s_gb, at(t, E - 1, EH + 1))
                sp.dma_start(gate_row[0:1, 0:E - 1 - EH, :], gT[3 * E + 1 + EH:4 * E, :]).then_inc(s_grow, 16)
                if exists(after(t, 3)):
                    wait_apart(sp, s_tp, at(t, MB, 2 * MB))
                    load_adj(after(t, 3))
                if exists(after(t, 2)):
                    wait_apart(sp, s_xn2, at(t, 1, 1))
                    load_x_nat(after(t, 2))
                if h == 0 and exists((b + 2, 0)):
                    wait_apart(sp, s_xn, b + 2)
                    load_x_perm(b + 2)
                wait_apart(sp, s_fin, at(t, 1, 2))
                sp.dma_start(out[b, h * TN:(h + 1) * TN, :].rearrange("(k p) d -> p k d", p=P), y[:, h]) \
                    .then_inc(s_out[h], 16)

            over_tiles(sp, tile)
            for h in range(2):
                sp.wait_ge(s_out[h], 16 * B + 16)

        @block.gpsimd
        def _(pool):
            nc.gpsimd.memset(ident[:, :], 0.0).then_inc(s_ident, 1)
            nc.gpsimd.memset(half_neg[:, :], -0.5).then_inc(s_ident, 1)
            pool.wait_ge(s_ident, 2)
            nc.gpsimd.affine_select(out=ident[:, :], in_=ident[:, :], compare_op=ALU.not_equal, fill=1.0,
                                    base=0, pattern=[[-1, P]], channel_multiplier=1).then_inc(s_ident, 1)

            def rsqrt1(b):
                pool.wait_ge(s_ve1, b + 1)
                nc.gpsimd.tensor_tensor(rstd1[:, :], ve1[:, :], half_neg[:, :], ALU.pow).then_inc(s_rstd1, 1)

            def xn_low(b):
                flat = "p m d -> p (m d)"
                pool.wait_ge(s_xnhi, b + 1)
                nc.gpsimd.tensor_tensor(xn_lo[:, :, :].rearrange(flat), x_perm[:, :, :].rearrange(flat),
                                        xn_hi[:, :, :].rearrange(flat).bitcast(F32), ALU.subtract) \
                    .then_inc(s_xn, 1)

            def rsqrt2(t):
                pool.wait_ge(s_ve2, at(t, 1, 1))
                nc.gpsimd.tensor_tensor(rstd2[:, :], ve2[:, :], half_neg[:, 0:KT], ALU.pow).then_inc(s_rstd2, 1)

            def broadcast_gates(t, e0, e1):
                wait_apart(pool, s_grow, at(t, 32, 16 if e0 == 1 else 32))
                for e in range(e0, e1):
                    nc.gpsimd.partition_broadcast(gate_all[:, e, :], gate_row[0:1, e - e0, :], P).then_inc(s_gb, 1)

            def adj_low(t, m0, m1):
                for m in range(m0, m1):
                    pool.wait_ge(s_adjhi, at(t, MB, m + 1))
                    nc.gpsimd.tensor_tensor(adj_lo[:, slot(t, m), :], adjT[:, m % RING, :],
                                            adj_hi[:, slot(t, m), :].bitcast(F32), ALU.subtract).then_inc(s_adjlo, 1)

            def h1_low(t, e):
                pool.wait_ge(s_h1e, at(t, E, e + 1))
                nc.gpsimd.tensor_tensor(h1e_lo[:, e % 2, :], h1e[:, e % 2, :], h1e_hi[:, e % 2, :].bitcast(F32),
                                        ALU.subtract).then_inc(s_h1lo["pool"], 1)

            def add_b2(t):
                b, h = t
                pool.wait_ge(s_xnat[h], b * 16 + 16)
                nc.gpsimd.tensor_tensor(x_nat[:, h], x_nat[:, h], b2_row[:, :].unsqueeze(1).broadcast_to([P, KT, P]),
                                        ALU.add).then_inc(s_xb, 1)

            def weight_low(i, hi, lo, whole):
                pool.wait_ge(s_whi, i + 1)
                nc.gpsimd.tensor_tensor(lo, whole, hi.bitcast(F32), ALU.subtract).then_inc(s_wlo, 1)

            pool.sem_inc(s_gb, 1)
            pool.sem_inc(s_adjlo, 1 + MB)
            rsqrt1(0)
            xn_low(0)
            weight_low(0, W1_hi[:, :], W1_lo[:, :], W1_raw)
            weight_low(1, rw1_hi[:, :], rw1_lo[:, :], rw1_raw)
            weight_low(2, e1_hi[:, :, :], e1_lo[:, :, :], e1_raw)
            weight_low(3, e2_hi[:, :, :], e2_lo[:, :, :], e2_raw)
            pool.wait_ge(s_eye, 1)
            add_diagonal(nc.gpsimd, (0, 1))
            pool.wait_ge(s_w, 16 * WEIGHT_LOADS)
            add_b2((0, 0))
            adj_low((0, 1), 0, 2)
            rsqrt2((0, 0))
            adj_low((0, 1), 2, MB - 1)
            rsqrt1(1)
            adj_low((0, 1), MB - 1, MB)

            def tile(t, front, prep):
                b, h = t
                p2 = after(t, 2)
                if prep:
                    add_diagonal(nc.gpsimd, p2)
                h1_low(t, 1)
                wait_apart(pool, s_h2e, at(t, E, 1))
                broadcast_gates(t, 1, 1 + EH)
                if front:
                    add_b2(after(t, 1))
                h1_low(t, 3)
                if prep:
                    adj_low(p2, 0, 1)
                if front:
                    rsqrt2(after(t, 1))
                broadcast_gates(t, 1 + EH, E)
                if h == 0 and prep:
                    xn_low(b + 1)
                if prep:
                    adj_low(p2, 1, 3)
                if h == 1 and exists((b + 2, 0)):
                    rsqrt1(b + 2)
                if prep:
                    adj_low(p2, 3, MB)

            over_tiles(pool, tile)

        def ln_stats(steps, last, bn, mv, ve, n):
            steps.then(last, apart=True)
            for k in range(n):
                last = nc.vector.bn_aggr(mv[:, k, :], bn[:, k, :])
            steps.then(last)
            return nc.vector.tensor_scalar(ve[:, :], mv[:, :, 1], LN_EPS, None, ALU.add)

        LN_STEPS = 2
        ROUTE_STEPS = 13

        @block.vector
        def _(dve):
            dve.sem_inc(s_h2e, 1)
            dve.sem_inc(s_fin, 1)
            nc.vector.memset(rw1_raw, 0.0).then_inc(s_clear, 1)
            nc.vector.memset(bias_rows[:, :], 0.0).then_inc(s_clear, 1)
            nc.vector.memset(rw2_sb[:, :], 0.0).then_inc(s_clear, 1)
            nc.vector.memset(gates[:, :, :], 0.0).then_inc(s_setup, 1)
            nc.vector.memset(cT_stack[:, :], 0.0).then_inc(s_setup, 1)
            nc.vector.memset(pr[:, :, :], -1.0).then_inc(s_setup, 1)
            for e in range(E):
                nc.vector.memset(numbers[:, e:e + 1], float(e)).then_inc(s_setup, 1)
            SETUP = 3 + E

            def transpose_adj(t, m0, m1):
                b, h = t
                for m in range(m0, m1):
                    if m == 0:
                        dve.wait_ge(s_diag, at(t, 2, 2))
                    if h == 1 or not in_first_graph(t):
                        dve.wait_ge(s_adjlo, at(t, MB, m + 2 - RING))
                    src = raw[:, h, 0:RB * QC].rearrange("p (k m j) -> p m k j", m=MB, j=32)[:, m]
                    nc.vector.transpose(adjT[:, m % RING, :].rearrange("p (k i) -> p k i", i=32), src) \
                        .then_inc(s_tp, 1)

            def ln1_stats(b, m0, m1):
                if m0 == 0:
                    dve.wait_ge(s_xp, b * (16 * Q) + 16 * Q)
                for m in range(m0, m1):
                    last = nc.vector.bn_stats(bn1[:, m, :], x_perm[:, m, :])
                return last

            def ln1_sums(b, last):
                ln_stats(Steps(dve, s_ln1, b * LN_STEPS), last, bn1, mv1, ve1, MB).then_inc(s_ve1, 1)

            def ln1_norm(b, m0, m1):
                if m0 == 0:
                    dve.wait_ge(s_rstd1, b + 1)
                for m in range(m0, m1):
                    last = nc.vector.tensor_scalar(x_perm[:, m, :], x_perm[:, m, :], mv1[:, m, 0:1],
                                                   rstd1[:, m:m + 1], ALU.subtract, ALU.mult)
                if m1 == MB:
                    last.then_inc(s_norm1, 1)

            def h_lo(t):
                dve.wait_ge(s_hhi, at(t, 1, 1))
                nc.vector.tensor_tensor(hT_lo[:, :], FA[:, :], hT_hi[:, :].bitcast(F32), ALU.subtract) \
                    .then_inc(s_hlo, 1)

            def x_lo(t):
                dve.wait_ge(s_xhi, at(t, 1, 1))
                nc.vector.tensor_tensor(xT_lo[:, t[1], :], FB[:, :], xT_hi[:, t[1], :].bitcast(F32),
                                        ALU.subtract).then_inc(s_xlo, 1)

            def residual(t):
                b, h = t
                dve.wait_ge(s_g2, at(t, 1, 1))
                dve.wait_ge(s_xb, at(t, 1, 1))
                steps = Steps(dve, s_ln2, at(t, LN_STEPS + 1))
                steps.then(nc.vector.tensor_tensor(x2[:, h].rearrange("p k d -> p (k d)"), FB[:, :],
                                                   x_nat[:, h].rearrange("p k d -> p (k d)"), ALU.add))

            def ln2_stats(t):
                for k in range(KT):
                    last = nc.vector.bn_stats(bn2[:, k, :], x2[:, t[1], k, :])
                steps = Steps(dve, s_ln2, at(t, LN_STEPS + 1, 1))
                ln_stats(steps, last, bn2, mv2, ve2, KT).then_inc(s_ve2, 1)
                assert steps.n == LN_STEPS

            def norm2(t):
                h = t[1]
                dve.wait_ge(s_rstd2, at(t, 1, 1))
                for k in range(KT):
                    last = nc.vector.tensor_scalar(xn2[:, k, :], x2[:, h, k, :], mv2[:, k, 0:1],
                                                   rstd2[:, k:k + 1], ALU.subtract, ALU.mult)
                last.then_inc(s_xn2, 1)

            def h1_low(t, e):
                dve.wait_ge(s_h1e, at(t, E, e + 1))
                nc.vector.tensor_tensor(h1e_lo[:, e % 2, :], h1e[:, e % 2, :], h1e_hi[:, e % 2, :].bitcast(F32),
                                        ALU.subtract).then_inc(s_h1lo["dve"], 1)

            def expert_gate(t, e):
                dve.wait_ge(s_z2, at(t, E, e + 1))
                if e == 0:
                    dve.wait_ge(s_g0, at(t, 1, 1))
                else:
                    dve.wait_ge(s_gb, at(t, E - 1, e + 1))
                if e >= 2:
                    dve.wait_ge(s_l3, at(t, E, e - 1))
                nc.vector.scalar_tensor_tensor(out=h2e[:, e % 2, :], in0=z2[e % 2][:, :],
                                               scalar=neg_eb2[:, e:e + 1], in1=gate_all[:, e, :],
                                               op0=ALU.max, op1=ALU.mult).then_inc(s_h2e, 1)

            def finish(t):
                b, h = t
                dve.wait_ge(s_ft, at(t, 1, 1))
                dve.wait_ge(s_out[h], b * 16 + 16)
                nc.vector.tensor_tensor(y[:, h].rearrange("p k d -> p (k d)"), FC[:, :],
                                        x2[:, h].rearrange("p k d -> p (k d)"), ALU.add).then_inc(s_fin, 1)

            def wide(v):
                return v.unsqueeze(2).broadcast_to([P, KT, E])

            def route(t, stats=None, norm=None):
                def beside(m0, m1):
                    if stats is not None:
                        ln1_stats(stats, m0, m1)
                    if norm is not None:
                        ln1_norm(norm, m0, m1)

                TT, v = nc.vector.tensor_tensor, nc.vector
                steps = Steps(dve, s_rs, at(t, ROUTE_STEPS))
                bias = rb2_row[:, :].unsqueeze(1).broadcast_to([P, KT, E])
                number = numbers[:, :].unsqueeze(1).broadcast_to([P, KT, E])
                dve.wait_ge(s_lg, at(t, 1, 1))
                steps.then(TT(lg[:, :, :], FB[:, 0:KT * E].rearrange("p (k e) -> p k e", e=E), bias, ALU.add),
                           beside=lambda: beside(0, 1))
                steps.then(v.reduce_max(mx[:, :], lg[:, :, :], AX))
                TT(lgd[:, :, :], lg[:, :, :], wide(mx[:, :]), ALU.subtract).then_inc(s_lgd, 1)
                beside(1, 3)
                dve.wait_ge(s_ex, at(t, 2, 1))
                steps.then(v.reduce_sum(sm[:, :], ex[:, :, :], AX), beside=lambda: beside(3, 4))
                steps.then(v.reciprocal(inv[:, :], sm[:, :]))
                steps.then(TT(pr[:, :, 0:E], ex[:, :, :], wide(inv[:, :]), ALU.mult), apart=True)
                for k in range(KT):
                    last = v.max(best[:, k, :], pr[:, k, :])
                steps.then(last)
                TT(dm[:, :], best[:, :, 1], best[:, :, 0], ALU.subtract).then_inc(s_dm, 1)
                for k in range(KT):
                    last = v.max_index(best_at[:, k, :], best[:, k, :], pr[:, k, :])
                steps.then(last)
                TT(top1[:, :, :], number, wide(best_at[:, :, 0]), ALU.is_equal)
                TT(top2[:, :, :], number, wide(best_at[:, :, 1]), ALU.is_equal)
                dve.wait_ge(s_ex, at(t, 2, 2))
                steps.then(v.tensor_scalar(den[:, :], ed[:, :], 1.0, None, ALU.add))
                steps.then(v.reciprocal(w1[:, :], den[:, :]))
                TT(g1[:, :, :], top1[:, :, :], wide(w1[:, :]), ALU.mult)
                steps.then(TT(w2[:, :], ed[:, :], w1[:, :], ALU.mult))
                steps.then(TT(g2[:, :, :], top2[:, :, :], wide(w2[:, :]), ALU.mult))
                steps.then(TT(gates[:, :, 3 * E:4 * E], g1[:, :, :], g2[:, :, :], ALU.add))
                steps.then(v.tensor_copy(gate_hi[:, :, :], gates[:, :, 3 * E:4 * E]))
                v.tensor_copy(gates[:, :, 0:E], gate_hi[:, :, :].bitcast(F32))
                v.tensor_copy(gates[:, :, 2 * E:3 * E], gate_hi[:, :, :].bitcast(F32))
                TT(gates[:, :, E:2 * E], gates[:, :, 3 * E:4 * E], gate_hi[:, :, :].bitcast(F32),
                   ALU.subtract).then_inc(s_gates, 1)
                assert steps.n == ROUTE_STEPS, steps.n

            ln1_sums(0, ln1_stats(0, 0, MB))
            dve.wait_ge(s_setup, SETUP)
            dve.wait_ge(s_ident, 3)
            dve.wait_ge(s_eps, 16)
            nc.vector.tensor_scalar(eps_col[:, :], eps_col[:, :], 1.0, None, ALU.add).then_inc(s_setup, 1)
            dve.wait_ge(s_setup, SETUP + 1)
            nc.vector.tensor_scalar(eps_eye[:, :, :].rearrange("p q j -> p (q j)"), ident[:, :], eps_col[:, 0:1],
                                    None, ALU.mult).then_inc(s_eye, 1)
            nc.vector.tensor_tensor(pick_first[:, :], ident[:, 0:1].broadcast_to([P, P]),
                                    ident[:, E:E + 1].broadcast_to([P, P]), ALU.add)
            ln1_norm(0, 0, MB)
            dve.wait_ge(s_eye, 1)
            add_diagonal(nc.vector, (0, 0))

            for m in range(MB + 1):
                if m < MB:
                    transpose_adj((0, 0), m, m + 1)
                if m >= 1:
                    dve.wait_ge(s_adjhi, m)
                    nc.vector.tensor_tensor(adj_lo[:, slot((0, 0), m - 1), :], adjT[:, (m - 1) % RING, :],
                                            adj_hi[:, slot((0, 0), m - 1), :].bitcast(F32), ALU.subtract) \
                        .then_inc(s_adjlo0, 1)

            dve.wait_ge(s_setup_pe, 1)
            nc.vector.tensor_copy(bias_cols[:, :], z2[0][:, 0:32]).then_inc(s_setup, 1)
            dve.wait_ge(s_setup, SETUP + 2)
            nc.vector.tensor_scalar(neg_eb2[:, :], eb2_col, -1.0, None, ALU.mult).then_inc(s_bias, 1)

            h_lo((0, 0))
            transpose_adj((0, 1), 0, RING)
            residual((0, 0))
            ln2_stats((0, 0))
            dve.wait_ge(s_setup_pe, 2)
            c_steps = Steps(dve, s_c, 0)
            c_steps.then(nc.vector.tensor_tensor(cT[:, :], z2[0][:, 0:E], eb3_col, ALU.add))
            c_steps.then(nc.vector.tensor_copy(cT_hi[:, :], cT[:, :]))
            nc.vector.tensor_tensor(cT_stack[:, 2 * E:3 * E], cT[:, :], cT_hi[:, :].bitcast(F32), ALU.subtract)
            nc.vector.tensor_copy(cT_stack[:, 0:E], cT_hi[:, :].bitcast(F32))
            nc.vector.tensor_copy(cT_stack[:, E:2 * E], cT_hi[:, :].bitcast(F32)).then_inc(s_c, 1)
            norm2((0, 0))
            transpose_adj((0, 1), RING, RING + 1)
            x_lo((0, 0))
            transpose_adj((0, 1), RING + 1, MB)
            dve.wait_ge(s_setup_pe, 3)
            nc.vector.tensor_copy(c_stack[:, :], z2[1][:, 0:P]).then_inc(s_c, 1)
            ln1_sums(1, ln1_stats(1, 0, MB))
            route((0, 0))
            h1_low((0, 0), 0)
            ln1_norm(1, 0, MB // 2)

            def tile(t, front, prep):
                b, h = t
                f, p2 = after(t, 1), after(t, 2)
                if prep:
                    transpose_adj(p2, 0, 1)
                if h == 0 and prep:
                    ln1_norm(b + 1, MB // 2, MB)
                if h == 1 and exists((b + 2, 0)):
                    stats_end = ln1_stats(b + 2, MB // 2, MB)
                if front:
                    h_lo(f)
                expert_gate(t, 0)
                if h == 1 and exists((b + 2, 0)):
                    ln1_sums(b + 2, stats_end)
                h1_low(t, 2)
                expert_gate(t, 1)
                if prep:
                    transpose_adj(p2, 1, 2)
                if prep:
                    transpose_adj(p2, 2, 3)
                if front:
                    residual(f)
                    ln2_stats(f)
                expert_gate(t, 2)
                h1_low(t, 4)
                if front:
                    norm2(f)
                expert_gate(t, 3)
                h1_low(t, 5)
                expert_gate(t, 4)
                if front:
                    x_lo(f)
                if prep:
                    transpose_adj(p2, 3, 4)
                expert_gate(t, 5)
                if prep:
                    transpose_adj(p2, 4, MB)
                if front:
                    more = exists((b + 2, 0))
                    route(f, stats=b + 2 if more and h == 0 else None, norm=b + 2 if more and h == 1 else None)
                    h1_low(f, 0)
                finish(t)

            over_tiles(dve, tile)

        @block.scalar
        def _(act):
            def adj_high(t, m0, m1):
                for m in range(m0, m1):
                    if m == 0 and not in_first_graph(t):
                        act.wait_ge(s_agg, at(t, 1, -1))
                    if m == OWN and (t[1] == 1 or not in_first_graph(t)):
                        act.wait_ge(s_agg, at(t, 1))
                    act.wait_ge(s_tp, at(t, MB, m + 1))
                    nc.scalar.activation(adj_hi[:, slot(t, m), :], adjT[:, m % RING, :], ACT.Copy).then_inc(s_adjhi, 1)

            def xn_high(b):
                act.wait_ge(s_norm1, b + 1)
                if not in_first_graph((b, 0)):
                    act.wait_ge(s_agg, b * 2)
                nc.scalar.activation(xn_hi[:, :, :].rearrange("p m d -> p (m d)"),
                                     x_perm[:, :, :].rearrange("p m d -> p (m d)"), ACT.Copy).then_inc(s_xnhi, 1)

            def h_hi(t):
                act.wait_ge(s_agg, at(t, 1, 1))
                nc.scalar.activation(hT_hi[:, :], FA[:, :], ACT.Copy).then_inc(s_hhi, 1)

            def h1(t):
                for c in range(NH):
                    act.wait_ge(s_g1, at(t, NH, c + 1))
                    nc.scalar.activation(h1T[:, c, :], (FB, FC)[c][:, :], ACT.Relu, bias=b1_col[:, c:c + 1]) \
                        .then_inc(s_h1, 1)

            def x_hi(t):
                act.wait_ge(s_tr2, at(t, 1, 1))
                nc.scalar.activation(xT_hi[:, t[1], :], FB[:, :], ACT.Copy).then_inc(s_xhi, 1)

            def router_hidden(t):
                act.wait_ge(s_rt, at(t, 1, 1))
                nc.scalar.activation(rhT[:, :], FC[:, :], ACT.Relu, bias=rb1_col[:, 0:1]).then_inc(s_rh, 1)

            def exp_logits(t):
                act.wait_ge(s_lgd, at(t, 1, 1))
                nc.scalar.activation(ex[:, :, :], lgd[:, :, :], ACT.Exp).then_inc(s_ex, 1)

            def exp_difference(t):
                act.wait_ge(s_dm, at(t, 1, 1))
                nc.scalar.activation(ed[:, :], dm[:, :], ACT.Exp).then_inc(s_ex, 1)

            def copy_gates(t):
                act.wait_ge(s_gt, at(t, 1, 1))
                nc.scalar.activation(gT_stack[:, :], FB[:, :], ACT.Copy).then_inc(s_gst, 1)
                act.wait_ge(s_gb, at(t, E - 1, 1))
                nc.scalar.activation(gT[:, :], FB[0:SEL, :], ACT.Copy).then_inc(s_gte, 1)

            def first_gate(t):
                act.wait_ge(s_pick, at(t, 1, 1))
                nc.scalar.activation(gate_all[:, 0, :], acc[:, :], ACT.Copy).then_inc(s_g0, 1)

            def expert_h1(t, e):
                act.wait_ge(s_z1, at(t, E, e + 1))
                if e >= 2:
                    act.wait_ge(s_z2, at(t, E, e - 1))
                nc.scalar.activation(h1e_hi[:, e % 2, :], z1[e % 2][:, :], ACT.Relu, bias=eb1_col[:, e:e + 1])
                nc.scalar.activation(h1e[:, e % 2, :], z1[e % 2][:, :], ACT.Relu, bias=eb1_col[:, e:e + 1]) \
                    .then_inc(s_h1e, 1)

            def copy_acc(t):
                act.wait_ge(s_acc, at(t, 1, 1))
                nc.scalar.activation(accT[:, :], acc[:, :], ACT.Copy).then_inc(s_acce, 1)

            def weight_high(hi, whole):
                nc.scalar.activation(hi, whole, ACT.Copy).then_inc(s_whi, 1)

            xn_high(0)
            adj_high((0, 0), 0, 4)
            act.wait_ge(s_wraw, 4 * 16)
            weight_high(W1_hi[:, :], W1_raw)
            weight_high(rw1_hi[:, :], rw1_raw)
            adj_high((0, 0), 4, 5)
            weight_high(e1_hi[:, :, :], e1_raw)
            adj_high((0, 0), 5, 6)
            weight_high(e2_hi[:, :, :], e2_raw)
            adj_high((0, 0), 6, MB)
            h_hi((0, 0))
            act.wait_ge(s_bias, 1)
            h1((0, 0))
            adj_high((0, 1), 0, RING)
            x_hi((0, 0))
            adj_high((0, 1), RING, RING + 1)
            router_hidden((0, 0))
            adj_high((0, 1), RING + 1, MB)
            exp_logits((0, 0))
            exp_difference((0, 0))
            expert_h1((0, 0), 0)
            expert_h1((0, 0), 1)

            def tile(t, front, prep):
                b, h = t
                f, p2 = after(t, 1), after(t, 2)
                copy_gates(t)
                if front:
                    h_hi(f)
                first_gate(t)
                expert_h1(t, 2)
                if front:
                    h1(f)
                if prep:
                    adj_high(p2, 0, 1)
                expert_h1(t, 3)
                if prep:
                    adj_high(p2, 1, 2)
                if h == 0 and prep:
                    xn_high(b + 1)
                if prep:
                    adj_high(p2, 2, 3)
                expert_h1(t, 4)
                expert_h1(t, 5)
                if front:
                    x_hi(f)
                if prep:
                    adj_high(p2, 3, 4)
                if front:
                    router_hidden(f)
                if prep:
                    adj_high(p2, 4, 6)
                copy_acc(t)
                if prep:
                    adj_high(p2, 6, 7)
                if front:
                    exp_logits(f)
                if prep:
                    adj_high(p2, 7, MB)
                if front:
                    exp_difference(f)
                    expert_h1(f, 0)
                    expert_h1(f, 1)

            over_tiles(act, tile)

        @block.tensor
        def _(pe):
            mm = nc.tensor.matmul

            def three_pass(dst, w_hi, w_lo, m_hi, m_lo, start=True, stop=True):
                mm(dst, w_lo, m_hi, start=start, stop=False)
                mm(dst, w_hi, m_lo, start=False, stop=False)
                return mm(dst, w_hi, m_hi, start=False, stop=stop)

            def aggregate(t, m0, m1):
                b, h = t
                if m0 == 0 and h == 0:
                    pe.wait_ge(s_xn, b + 1)
                for m in range(m0, m1):
                    if in_first_graph(t) and h == 0:
                        pe.wait_ge(s_adjlo0, m + 1)
                    else:
                        pe.wait_ge(s_adjlo, at(t, MB, m + 2))
                    last = three_pass(FA[:, :], xn_hi[:, m, :], xn_lo[:, m, :], adj_hi[:, slot(t, m), :],
                                      adj_lo[:, slot(t, m), :], start=(m == 0), stop=(m == MB - 1))
                if m1 == MB:
                    last.then_inc(s_agg, 1)

            def gin1(t):
                pe.wait_ge(s_hlo, at(t, 1, 1))
                for c in range(NH):
                    w = slice(c * P, (c + 1) * P)
                    three_pass((FB, FC)[c][:, :], W1_hi[:, w], W1_lo[:, w], hT_hi[:, :], hT_lo[:, :]) \
                        .then_inc(s_g1, 1)

            def gin2(t):
                for k in range(KT):
                    n = slice(k * P, (k + 1) * P)
                    for c in range(NH):
                        if k == 0:
                            pe.wait_ge(s_h1, at(t, NH, c + 1))
                        last = mm(FB[:, n], h1T[:, c, n], W2_sb[:, c, :], start=(c == 0), stop=(c == NH - 1))
                last.then_inc(s_g2, 1)

            def transposes(dst, src):
                for k in range(KT):
                    last = nc.tensor.transpose(dst[:, k * P:(k + 1) * P], src(k), ident[:, :])
                return last

            def xn2_transposed(t):
                pe.wait_ge(s_xn2, at(t, 1, 1))
                transposes(FB, lambda k: xn2[:, k, :]).then_inc(s_tr2, 1)

            def router1(t):
                h = t[1]
                pe.wait_ge(s_xlo, at(t, 1, 1))
                three_pass(FC[:, :], rw1_hi[:, :], rw1_lo[:, :], xT_hi[:, h, :], xT_lo[:, h, :]).then_inc(s_rt, 1)

            def logits(t):
                pe.wait_ge(s_rh, at(t, 1, 1))
                for k in range(KT):
                    last = mm(FB[:, k * E:(k + 1) * E], rhT[:, k * P:(k + 1) * P], rw2_sb[:, :],
                              start=True, stop=True)
                last.then_inc(s_lg, 1)

            def gates_transposed(t):
                pe.wait_ge(s_gates, at(t, 1, 1))
                transposes(FB, lambda k: gates[:, k, :]).then_inc(s_gt, 1)

            def spread_first_gate(t):
                pe.wait_ge(s_gst, at(t, 1, 1))
                mm(acc[:, :], pick_first[:, :], gT_stack[:, :], start=True, stop=True).then_inc(s_pick, 1)

            def expert1(t, e):
                h = t[1]
                if e >= 2:
                    pe.wait_ge(s_h1e, at(t, E, e - 1))
                three_pass(z1[e % 2][:, :], e1_hi[:, e, :], e1_lo[:, e, :], xT_hi[:, h, :], xT_lo[:, h, :]) \
                    .then_inc(s_z1, 1)

            def expert2(t, e):
                semaphore, value = h1_low_done(t, e)
                pe.wait_ge(semaphore, value)
                if e >= 2:
                    pe.wait_ge(s_h2e, at(t, E, e))
                three_pass(z2[e % 2][:, :], e2_hi[:, e, :], e2_lo[:, e, :], h1e_hi[:, e % 2, :],
                           h1e_lo[:, e % 2, :]).then_inc(s_z2, 1)

            def expert3(t, e):
                pe.wait_ge(s_h2e, at(t, E, e + 2))
                mm(acc[:, :], e3_sb[:, e, :], h2e[:, e % 2, :], start=(e == 0), stop=False).then_inc(s_l3, 1)

            def expert_biases(t):
                pe.wait_ge(s_gst, at(t, 1, 1))
                mm(acc[:, :], c_stack[:, :], gT_stack[:, :], start=False, stop=True).then_inc(s_acc, 1)

            def acc_rows(t):
                pe.wait_ge(s_acce, at(t, 1, 1))
                transposes(FC, lambda k: accT[:, k * P:(k + 1) * P]).then_inc(s_ft, 1)

            aggregate((0, 0), 0, MB)
            pe.wait_ge(s_ident, 3)
            pe.wait_ge(s_brow, 16 * BIAS_LOADS)
            nc.tensor.transpose(z2[0][:, 0:32], bias_rows[:, :], ident[0:32, 0:32]).then_inc(s_setup_pe, 1)
            pe.wait_ge(s_wlo, 1)
            gin1((0, 0))
            pe.wait_ge(s_w, 16 * WEIGHT_LOADS)
            gin2((0, 0))
            pe.wait_ge(s_bias, 1)
            for e in range(E):
                last = mm(z2[0][:, e:e + 1], e3_sb[:, e, :], eb2_col[:, e:e + 1], start=True, stop=True)
            last.then_inc(s_setup_pe, 1)
            aggregate((0, 1), 0, 2)
            pe.wait_ge(s_c, 3)
            nc.tensor.transpose(z2[1][:, 0:P], cT_stack[:, :], ident[:, :]).then_inc(s_setup_pe, 1)
            xn2_transposed((0, 0))
            aggregate((0, 1), 2, 4)
            pe.wait_ge(s_wlo, 2)
            router1((0, 0))
            logits((0, 0))
            pe.wait_ge(s_wlo, 3)
            expert1((0, 0), 0)
            expert1((0, 0), 1)
            aggregate((0, 1), 4, MB - 1)
            pe.wait_ge(s_c, 4)
            pe.wait_ge(s_wlo, 4)

            def tile(t, front, prep):
                f = after(t, 1)
                gates_transposed(t)
                if front:
                    aggregate(f, MB - 1, MB)
                expert2(t, 0)
                spread_first_gate(t)
                expert1(t, 2)
                expert2(t, 1)
                if front:
                    pe.wait_ge(s_fin, at(t, 1, 1))
                    pe.wait_ge(s_gte, at(t, 1, 1))
                    gin1(f)
                expert1(t, 3)
                if front:
                    gin2(f)
                expert3(t, 0)
                expert2(t, 2)
                expert1(t, 4)
                expert3(t, 1)
                expert2(t, 3)
                expert1(t, 5)
                expert3(t, 2)
                expert2(t, 4)
                if front:
                    xn2_transposed(f)
                expert3(t, 3)
                expert2(t, 5)
                expert3(t, 4)
                if front:
                    router1(f)
                expert3(t, 5)
                expert_biases(t)
                if front:
                    logits(f)
                    expert1(f, 0)
                    expert1(f, 1)
                acc_rows(t)
                if prep:
                    aggregate(after(t, 2), 0, MB - 1)

            over_tiles(pe, tile)


_INS = ["x", "adj", "L0_gnn_eps", "L0_gnn_W1", "L0_gnn_b1", "L0_gnn_W2", "L0_gnn_b2",
        "L0_ffn_router_w1", "L0_ffn_router_b1", "L0_ffn_router_w2", "L0_ffn_router_b2",
        "L0_ffn_expert_w1", "L0_ffn_expert_b1", "L0_ffn_expert_w2", "L0_ffn_expert_b2",
        "L0_ffn_expert_w3", "L0_ffn_expert_b3"]


def kernel(**inputs):
    import numpy as np
    import concourse.bacc as bacc
    from concourse.bass_utils import run_bass_kernel_spmd

    nc = bacc.Bacc("TRN2", target_bir_lowering=False, num_devices=1)
    arrays, args = {}, []
    for name in _INS:
        a = np.ascontiguousarray(inputs[name])
        arrays[name] = a
        args.append(nc.dram_tensor(name, a.shape, mybir.dt.from_np(a.dtype), kind="ExternalInput").ap())
    y = nc.dram_tensor("y_out", arrays["x"].shape, F32, kind="ExternalOutput").ap()
    build(nc, *args, y)
    r = run_bass_kernel_spmd(nc, [arrays], core_ids=[0])
    return r.results[0]["y_out"]
```
